# Optimizing a Trainium2 kernel written in Bass

```python
import numpy as np
import jax
import jax.numpy as jnp

def _softmax(x, axis=-1):
    return jax.nn.softmax(x, axis=axis)

def _gelu(x):
    return jax.nn.gelu(x, approximate=True)

def _silu(x):
    return jax.nn.silu(x)

def _sigmoid(x):
    return jax.nn.sigmoid(x)

def _layernorm(x, axis=-1, eps=1e-05):
    m = jnp.mean(x, axis=axis, keepdims=True)
    v = jnp.var(x, axis=axis, keepdims=True)
    return (x - m) / jnp.sqrt(v + eps)

def _scatter_add(tgt, idx, src, axis=0):
    return tgt.at[idx].add(src)

def _segment_sum(src, seg, n):
    return jax.ops.segment_sum(src, seg, n)
kernel_name = 'mk_adaln_d1_jaxref_r4_a0b2dc'

def setup_inputs(seed: int=0):
    np.random.seed(seed)
    _w = jnp.asarray

    def _L0_attn_setup():
        import jax, jax.numpy as jnp
        import numpy as np
        N_Q_HEAD = 32
        N_KV_HEAD = 8
        N_EMBD = 1024
        B, T = (2, 512)
        key = jax.random.key(seed)
        ks = jax.random.split(key, 5)
        s = 0.02
        return {'x': jax.random.normal(ks[0], (B, T, N_EMBD), dtype=jnp.float32), 'Wq': jax.random.normal(ks[1], (N_EMBD, N_EMBD), dtype=jnp.float32) * s, 'Wk': jax.random.normal(ks[2], (N_EMBD // (N_Q_HEAD // N_KV_HEAD), N_EMBD), dtype=jnp.float32) * s, 'Wv': jax.random.normal(ks[3], (N_EMBD // (N_Q_HEAD // N_KV_HEAD), N_EMBD), dtype=jnp.float32) * s, 'Wo': jax.random.normal(ks[4], (N_EMBD, N_EMBD), dtype=jnp.float32) * s, 'bo': jnp.zeros((N_EMBD,), dtype=jnp.float32)}
    _L0_attn_in = _L0_attn_setup()

    def _L0_ffn_setup():
        import jax, jax.numpy as jnp
        import numpy as np
        HIDDEN = 1024
        INTER = 2752

        def _ternary_quantize(w):
            scale = jnp.mean(jnp.abs(w))
            return jnp.clip(jnp.round(w / scale), -1.0, 1.0) * scale
        key = jax.random.key(seed)
        kx, kg, ku, kd = jax.random.split(key, 4)
        x = jax.random.normal(kx, (2, 512, HIDDEN), dtype=jnp.float32)
        w_gate = _ternary_quantize(jax.random.normal(kg, (INTER, HIDDEN), dtype=jnp.float32) * 0.02)
        w_up = _ternary_quantize(jax.random.normal(ku, (INTER, HIDDEN), dtype=jnp.float32) * 0.02)
        w_down = _ternary_quantize(jax.random.normal(kd, (HIDDEN, INTER), dtype=jnp.float32) * 0.02)
        return {'x': x, 'w_gate': w_gate, 'w_up': w_up, 'w_down': w_down}
    _L0_ffn_in = _L0_ffn_setup()
    _L0_c = _w((lambda *s: np.random.randn(*s).astype(np.float32) * 0.05)(1, 1024))
    _L0_wmod = _w((lambda *s: np.random.randn(*s).astype(np.float32) * 0.05)(1024, 6 * 1024) * 1024 ** (-0.5))
    _d = {'L0_attn_x': _L0_attn_in['x'], 'L0_attn_Wq': _L0_attn_in['Wq'], 'L0_attn_Wk': _L0_attn_in['Wk'], 'L0_attn_Wv': _L0_attn_in['Wv'], 'L0_attn_Wo': _L0_attn_in['Wo'], 'L0_attn_bo': _L0_attn_in['bo'], 'L0_ffn_w_gate': _L0_ffn_in['w_gate'], 'L0_ffn_w_up': _L0_ffn_in['w_up'], 'L0_ffn_w_down': _L0_ffn_in['w_down'], 'L0_c': _L0_c, 'L0_wmod': _L0_wmod}
    _x0 = _d['L0_attn_x']
    _d['L0_attn_x'] = jax.random.normal(jax.random.fold_in(jax.random.key(seed), 1), (1, 2048, 1024), dtype=_x0.dtype)
    del _x0
    return _d

def reference(L0_attn_x, L0_attn_Wq, L0_attn_Wk, L0_attn_Wv, L0_attn_Wo, L0_attn_bo, L0_ffn_w_gate, L0_ffn_w_up, L0_ffn_w_down, L0_c, L0_wmod):

    def _L0_attn_ref(x, Wq, Wk, Wv, Wo, bo):
        import jax, jax.numpy as jnp
        import numpy as np
        N_Q_HEAD = 32
        N_KV_HEAD = 8
        N_EMBD = 1024
        B, T = (2, 512)
        b, t, e = x.shape
        h_kv = N_KV_HEAD
        g = N_Q_HEAD // N_KV_HEAD
        d = e // N_Q_HEAD
        q = (x @ Wq.T).reshape(b, t, h_kv, g, d).transpose(0, 2, 3, 1, 4)
        k = (x @ Wk.T).reshape(b, t, h_kv, d).transpose(0, 2, 1, 3)
        v = (x @ Wv.T).reshape(b, t, h_kv, d).transpose(0, 2, 1, 3)
        scale = jnp.sqrt(jnp.asarray(d, dtype=x.dtype))
        att = jnp.einsum('bhgqd,bhkd->bhgqk', q, k) / scale
        att = jax.nn.softmax(att, axis=-1)
        y = jnp.einsum('bhgqk,bhkd->bhgqd', att, v)
        y = y.transpose(0, 3, 1, 2, 4).reshape(b, t, e)
        return y @ Wo.T + bo

    def _L0_ffn_ref(x, w_gate, w_up, w_down):
        import jax, jax.numpy as jnp
        import numpy as np
        HIDDEN = 1024
        INTER = 2752

        def _ternary_quantize(w):
            scale = jnp.mean(jnp.abs(w))
            return jnp.clip(jnp.round(w / scale), -1.0, 1.0) * scale
        xf = x.astype(jnp.float32) / 128.0
        gate = jnp.einsum('bsh,ih->bsi', xf, w_gate)
        up = jnp.einsum('bsh,ih->bsi', xf, w_up)
        inter = jax.nn.silu(gate) * up
        inter_q = jnp.trunc(jnp.clip(inter * 128.0, -128.0, 127.0)).astype(jnp.int8)
        down = jnp.einsum('bsi,hi->bsh', inter_q.astype(jnp.float32), w_down)
        out = jnp.trunc(jnp.clip(down * 128.0, -128.0, 127.0)).astype(jnp.int8)
        return out
    x = L0_attn_x
    mod = (_silu(L0_c) @ L0_wmod).reshape(L0_c.shape[0], 6, 1, -1)
    sa, ca, ga, sb, cb, gb = (mod[:, 0], mod[:, 1], mod[:, 2], mod[:, 3], mod[:, 4], mod[:, 5])
    ga = (2 * (ga >= 0) - 1) * jnp.maximum(jnp.abs(ga), 0.25)
    gb = (2 * (gb >= 0) - 1) * jnp.maximum(jnp.abs(gb), 0.25)
    h = _layernorm(x, axis=-1) * (1 + ca) + sa
    x = x + ga * _L0_attn_ref(h, L0_attn_Wq, L0_attn_Wk, L0_attn_Wv, L0_attn_Wo, L0_attn_bo)
    h = _layernorm(x, axis=-1) * (1 + cb) + sb
    x = x + gb * _L0_ffn_ref(h, L0_ffn_w_gate, L0_ffn_w_up, L0_ffn_w_down)
    return x

_drawn_inputs = setup_inputs


def setup_inputs(seed=0):
    import zlib

    import numpy as np

    out = dict(_drawn_inputs(seed))
    spreads = {'L0_attn_bo': (0.0, 1.983)}
    factors = {'L0_attn_Wq': 8.0, 'L0_attn_Wk': 8.0, 'L0_attn_Wv': 8.0, 'L0_attn_Wo': 8.0}
    for name, (base, spread) in spreads.items():
        noise = np.random.default_rng([zlib.crc32(name.encode()), seed]).standard_normal(out[name].shape)
        drawn = base * np.exp(spread * noise) if base else spread * noise
        out[name] = jnp.asarray(drawn.astype(out[name].dtype))
    for name, factor in factors.items():
        out[name] = (out[name] * factor).astype(out[name].dtype)
    return out
```

```python
import concourse.bass as bass
from concourse import mybir
from contextlib import ExitStack

F32 = mybir.dt.float32
F32R = mybir.dt.float32r
I8 = mybir.dt.int8
ALU = mybir.AluOpType
ACT = mybir.ActivationFunctionType
AX = mybir.AxisListType

P = 128
T = 2048
D = 1024
FT = D // P
TT = T // P
NB = 512
QB = T // NB
HQ, HKV, DH = 32, 8, 32
GH = HQ // HKV
INTER = 2752
IT = -(-INTER // P)
LASTI = INTER - (IT - 1) * P
EPS = 1e-5
INV_SQRT_DH = float(DH) ** -0.5
RNE = 1.5 * 2.0 ** 23

TERMS = ((0, 0), (0, 1), (1, 0))


HALF_W = FT * P
QW = D // 4
SHARED = max(6 * HALF_W, IT * QW)


def overlay(nc, stack, *views):
    out = []
    for i, (name, shape, dt) in enumerate(views):
        one = nc.sbuf_tensor(name, shape, dt)
        if i + 1 < len(views):
            with one as tensor:
                out.append(tensor)
        else:
            out.append(stack.enter_context(one))
    return out


class Links:

    def __init__(self, eng, sem, per_round=0):
        self.eng, self.sem, self.per_round = eng, sem, per_round
        self.base, self.n = 0, 0

    def at(self, rnd):
        assert self.per_round == 0 or self.n in (0, self.per_round), (self.n, self.per_round)
        self.base, self.n = rnd * self.per_round, 0

    def link(self, ins):
        self.n += 1
        ins.then_inc(self.sem, 1)
        self.eng.wait_ge(self.sem, self.base + self.n)


def rsqrt_steps(nc, v, ln, mv, s, sqrt_in, sqrt_out, nth):
    nc.vector.tensor_scalar_add(s[:, 0:1], mv[:, 1:2], EPS).then_inc(sqrt_in, 1)
    v.wait_ge(sqrt_in, nth)
    v.wait_ge(sqrt_out, nth)
    ln.link(nc.vector.reciprocal(s[:, 2:3], s[:, 1:2]))
    ln.link(nc.vector.tensor_tensor(s[:, 3:4], s[:, 2:3], s[:, 2:3], ALU.mult))
    ln.link(nc.vector.tensor_tensor(s[:, 3:4], s[:, 3:4], s[:, 0:1], ALU.mult))
    ln.link(nc.vector.tensor_scalar(s[:, 3:4], s[:, 3:4], -0.5, 1.5, ALU.mult, ALU.add))
    ln.link(nc.vector.tensor_tensor(s[:, 4:5], s[:, 2:3], s[:, 3:4], ALU.mult))


def stage_modulation_and_qkv(nc, ctx, c, wmod, x, wq_t, wk_t, wv_t, mod_dram, q_dram, k_dram, v_dram, modT, ident):
    MQ, MK, MV = HQ * DH // P, HKV * DH // P, HKV * DH // P
    MT = MQ + MK
    MW = MT + MV
    VW = HKV * DH
    BT = NB // P
    QKB = 3
    AHEAD = 4
    NG, GW = 3, 4 * NB
    NR = 5
    with ExitStack() as st:
        def sb(name, shape, dt=F32):
            return st.enter_context(nc.sbuf_tensor("qkv_" + name, shape, dt))

        def pb(name, width=NB):
            return st.enter_context(nc.psum_tensor("qkv_" + name, [P, width], F32))

        def sem(name):
            return st.enter_context(nc.semaphore("qkv_" + name))

        w = [sb(f"wqkv_{n}", [P, MW, FT, P], F32R) for n in ("hi", "lo")]
        wraws = sb("wqkv_raw", [P, 2, FT, P])
        wraw = [wraws[:, i] for i in range(2)]
        hT_1 = [overlay(nc, st, (f"qkv_wmod_{n}", [P, 2, GW], F32), (f"qkv_hT1_{n}", [P, FT, NB], F32R))
                for n in ("hi", "lo")]
        hT = [[sb(f"hT0_{n}", [P, FT, NB], F32R) for n in ("hi", "lo")], [i[1] for i in hT_1]]
        xt = [sb(f"x_tile{i}", [P, D]) for i in range(2)]
        stats = [sb(f"ln_stats{i}", [P, 12]) for i in range(2)]
        mv = [sb(f"ln_mv{i}", [P, 2]) for i in range(2)]
        s = [sb(f"ln_s{i}", [P, 8]) for i in range(2)]
        aff = [sb(f"h_affine{i}", [P, FT, P]) for i in range(2)]
        qko = [[sb(f"qk_out{i}_{n}", [P, NB], F32R) for n in ("hi", "lo")] for i in range(2)]
        vo = [sb(f"v_out{i}", [P, VW]) for i in range(2)]
        ccol, cwork = sb("c_col", [P, FT]), sb("c_work", [P, 3, FT])
        ones, crep = sb("ones_32", [P, 32]), sb("silu_c_rep", [P, FT, 32])
        rows = sb("mod_rows", [P, NB])
        wmod_own = sb("wmod", [P, GW])
        wmod_0 = [hT_1[i // 2][0][:, i % 2] for i in range(NR - 1)] + [wmod_own[:]]
        wmod_12 = [wraws[:].rearrange("p a k c -> p (a k c)"), wmod_own[:]]
        tr = pb("h_T", 2 * NB)
        qkp = [pb(f"qk_acc{i}") for i in range(QKB)]
        vp = [pb(f"v_acc{i}") for i in range(2)]
        modp = pb("mod_acc")

        def transposed(t, f):
            if t in (1, 2):
                bank = ((qkp[0], qkp[1]), (qkp[2], vp[0]))[t - 1][f * P // NB]
                return bank[:, f * P % NB:f * P % NB + P]
            return tr[:, f * P:(f + 1) * P]


        x_loaded, w_loaded = [sem(f"x_loaded{i}") for i in range(2)], [sem(f"w_loaded{i}") for i in range(2)]
        w_hi, w_split = sem("w_hi"), sem("w_split")
        var_done, root_done, xn_done = sem("var_done"), sem("root_done"), sem("xn_done")
        tr_done, aff_done, h_hi, h_split = sem("tr_done"), sem("aff_done"), sem("h_hi"), sem("h_split")
        qk_acc, qk_hi, qk_evac, qk_stored = sem("qk_acc"), sem("qk_hi"), sem("qk_evac"), [sem(f"qk_stored{i}") for i in range(2)]
        v_acc, v_evac, v_stored = sem("v_acc"), sem("v_evac"), [sem(f"v_stored{i}") for i in range(2)]
        c_loaded, exp_c_done, crep_done = sem("c_loaded"), sem("exp_c_done"), sem("silu_c_done")
        wmod_loaded0, wmod_loaded = [sem(f"wmod0_loaded{i}") for i in range(NR)], [sem(f"wmod_loaded{i}") for i in range(2)]
        mod_used, mod_rows, mod_T, mod_done = sem("wmod_used"), sem("mod_rows_done"), sem("mod_T_done"), sem("mod_done")
        row_stored, ident_zero, ident_done = sem("mod_row_stored"), sem("ident_zeroed"), sem("ident_done")
        dve = sem("qkv_dve_links")
        x_view = x.rearrange("a (t p) d -> (a t) p d", p=P)
        w_src = [wq_t[m] for m in range(MQ)] + [wk_t[m] for m in range(MK)] + [wv_t[m] for m in range(MV)]
        wmod_view = wmod.rearrange("(k p) (g n) -> g k p n", p=P, n=GW)
        qk_dst = [q_dram[:, m * P:(m + 1) * P, :] for m in range(MQ)]
        qk_dst += [k_dram[:, m * P:(m + 1) * P, :] for m in range(MK)]
        block = st.enter_context(nc.Block())

        def mod_place(b, m):
            return (b - 1) * FT + m if 1 <= b < NG and 0 <= m < FT else None

        @block.sync
        def _(sp):
            def load_x(t):
                if t >= 2:
                    sp.wait_ge(tr_done, t - 1)
                sp.dma_start(xt[t % 2][:], x_view[t]).then_inc(x_loaded[t % 2], 16)

            def load_wmod(k):
                if k >= NR:
                    sp.wait_ge(mod_used, k - NR + 1)
                sp.dma_start(wmod_0[k % NR], wmod_view[0, k]).then_inc(wmod_loaded0[k % NR], 16)

            sp.dma_start(ccol[:], c.rearrange("a (t p) -> p (a t)", p=P), allow_slow_non_contiguous=True).then_inc(c_loaded, 16)
            for k in range(FT):
                load_wmod(k)
                if k in (0, 1, 4, 6):
                    load_x((0, 1, 4, 6).index(k))
            for t in range(BT, TT):
                load_x(t)
                if t % BT == BT - 1 and t // BT >= 2:
                    g = t // BT - 1
                    sp.wait_ge(mod_rows, g + 1)
                    for j in ((0, 1), (2, 3))[g - 1]:
                        sp.dma_start(mod_dram[g * GW + j * NB:g * GW + (j + 1) * NB].rearrange("(a n) -> a n", a=1),
                                     rows[32 * j:32 * j + 1, :]).then_inc(row_stored, 16)
            sp.wait_ge(row_stored, 16 * 4)

        @block.gpsimd
        def _(pool):
            nc.gpsimd.memset(ident[:], 0.0).then_inc(ident_zero, 1)
            pool.wait_ge(ident_zero, 1)
            nc.gpsimd.affine_select(out=ident[:], in_=ident[:], compare_op=ALU.not_equal, fill=1.0,
                                    base=0, pattern=[[-1, P]], channel_multiplier=1).then_inc(ident_done, 1)

            def load_w(m):
                if m >= 2:
                    pool.wait_ge(w_split, m - 1)
                pool.dma_start(wraw[m % 2], w_src[m]).then_inc(w_loaded[m % 2], 16)

            for m in range(AHEAD + 2):
                load_w(m)
            for b in range(QB):
                for m in range(MT):
                    cc = b * MT + m
                    pool.wait_ge(qk_evac, cc + 1)
                    for n in range(2):
                        pool.dma_start(qk_dst[m][n, :, b * NB:(b + 1) * NB].bitcast(F32),
                                       qko[cc % 2][n][:].bitcast(F32)).then_inc(qk_stored[cc % 2], 16)
                    if b == 0 and m + AHEAD + 2 < MW:
                        load_w(m + AHEAD + 2)
                    i = mod_place((cc + 2) // MT, (cc + 2) % MT)
                    if i is not None:
                        if i == 0:
                            pool.wait_ge(w_split, MW)
                        elif i == 1:
                            pool.wait_ge(mod_used, FT)
                        else:
                            pool.wait_ge(mod_used, FT + i - 1)
                        pool.dma_start(wmod_12[i % 2], wmod_view[1 + i // FT, i % FT]).then_inc(wmod_loaded[i % 2], 16)
            for i in range(2):
                pool.wait_ge(qk_stored[i], 32 * QB * MT // 2)

        @block.scalar
        def _(act):
            def weights_hi(m):
                act.wait_ge(w_loaded[m % 2], 16 * (m // 2 + 1))
                nc.scalar.copy(w[0][:, m], wraw[m % 2]).then_inc(w_hi, 1)

            def root(t):
                act.wait_ge(var_done, t + 1)
                nc.scalar.activation(s[t % 2][:, 1:2], s[t % 2][:, 0:1], ACT.Sqrt).then_inc(root_done, 1)

            def affine(t):
                act.wait_ge(tr_done, t + 1)
                if t >= 2:
                    act.wait_ge(h_split, t - 1)
                for f in range(FT):
                    ins = nc.scalar.activation(aff[t % 2][:, f, :], transposed(t, f), ACT.Identity,
                                               scale=modT[:, 8 + f:9 + f], bias=modT[:, f:f + 1])
                ins.then_inc(aff_done, 1)

            def v_out(t):
                act.wait_ge(v_acc, t + 1)
                if t >= 2:
                    act.wait_ge(v_stored[t % 2], 16 * (t // 2))
                nc.scalar.copy(vo[t % 2][:], vp[t % 2][:, 0:VW]).then_inc(v_evac, 1)
                act.wait_ge(v_evac, t + 1)
                act.dma_start(v_dram[t * P:(t + 1) * P, :], vo[t % 2][:]).then_inc(v_stored[t % 2], 16)

            act.wait_ge(c_loaded, 16)
            nc.scalar.activation(cwork[:, 0, :], ccol[:], ACT.Exp, scale=-1.0).then_inc(exp_c_done, 1)
            root(0)
            root(1)
            weights_hi(0)
            weights_hi(1)
            root(2)
            root(3)
            act.wait_ge(mod_done, 1)
            affine(0)
            affine(1)
            affine(2)
            weights_hi(2)
            affine(3)
            weights_hi(3)
            for b in range(QB):
                for t in range(BT):
                    if b == 0:
                        weights_hi(AHEAD + 2 * t)
                        weights_hi(AHEAD + 2 * t + 1)
                    if b + 1 < QB:
                        root((b + 1) * BT + t)
                        affine((b + 1) * BT + t)
                for t in range(BT):
                    v_out(b * BT + t)
            for i in range(2):
                act.wait_ge(v_stored[i], 16 * TT // 2)

        @block.vector
        def _(v):
            ln = Links(v, dve)

            def weights_lo(m):
                v.wait_ge(w_hi, m + 1)
                nc.vector.tensor_tensor(w[1][:, m], wraw[m % 2], w[0][:, m].bitcast(F32),
                                        ALU.subtract).then_inc(w_split, 1)

            def norm_tile(t):
                j = t % 2
                v.wait_ge(x_loaded[j], 16 * (t // 2 + 1))
                ln.link(nc.vector.bn_stats(stats[j][:, 0:6], xt[j][:, 0:NB]))
                ln.link(nc.vector.bn_stats(stats[j][:, 6:12], xt[j][:, NB:D]))
                ln.link(nc.vector.bn_aggr(mv[j][:], stats[j][:]))
                rsqrt_steps(nc, v, ln, mv[j], s[j], var_done, root_done, t + 1)
                nc.vector.tensor_scalar(xt[j][:], xt[j][:], mv[j][:, 0:1], s[j][:, 4:5],
                                        ALU.subtract, ALU.mult).then_inc(xn_done, 1)

            def split_tile(t):
                b, cols = t // BT, slice(t % BT * P, (t % BT + 1) * P)
                v.wait_ge(aff_done, t + 1)
                if b >= 2:
                    v.wait_ge(v_acc, BT * (b - 1))
                nc.vector.tensor_copy(hT[b % 2][0][:, :, cols], aff[t % 2][:]).then_inc(h_hi, 1)
                v.wait_ge(h_hi, t + 1)
                nc.vector.tensor_tensor(hT[b % 2][1][:, :, cols], aff[t % 2][:], hT[b % 2][0][:, :, cols].bitcast(F32),
                                        ALU.subtract).then_inc(h_split, 1)

            def qk_out(c):
                v.wait_ge(qk_acc, c + 1)
                if c >= 2:
                    v.wait_ge(qk_stored[c % 2], 32 * (c // 2))
                nc.vector.tensor_copy(qko[c % 2][0][:], qkp[c % QKB][:]).then_inc(qk_hi, 1)
                v.wait_ge(qk_hi, c + 1)
                nc.vector.tensor_tensor(qko[c % 2][1][:], qkp[c % QKB][:], qko[c % 2][0][:].bitcast(F32),
                                        ALU.subtract).then_inc(qk_evac, 1)

            def mod_rows_out(g):
                v.wait_ge(mod_used, FT * (g + 1))
                if g == 2:
                    v.wait_ge(row_stored, 32)
                nc.vector.tensor_copy(rows[:], modp[:]).then_inc(mod_rows, 1)

            def mod_columns(g):
                v.wait_ge(mod_T, g + 1)
                cols = modT[:, g * 16:(g + 1) * 16].rearrange("p (j c) -> p c j", c=4)
                ins = nc.vector.tensor_copy(cols, modp[:].rearrange("p (c j r) -> p c j r", c=4, r=32)[:, :, :, 0])
                scale = {0: 8, 2: 32}.get(g)
                if scale is not None:
                    ln.link(ins)
                    ins = nc.vector.tensor_scalar_add(modT[:, scale:scale + 8], modT[:, scale:scale + 8], 1.0)
                ins.then_inc(mod_done, 1)

            ln.link(nc.vector.memset(ones[:], 1.0))
            v.wait_ge(exp_c_done, 1)
            ln.link(nc.vector.tensor_scalar_add(cwork[:, 1, :], cwork[:, 0, :], 1.0))
            ln.link(nc.vector.reciprocal(cwork[:, 2, :], cwork[:, 1, :]))
            ln.link(nc.vector.tensor_tensor(cwork[:, 0, :], cwork[:, 2, :], ccol[:], ALU.mult))
            for t in range(FT):
                last = nc.vector.tensor_scalar(crep[:, t, :], ones[:], cwork[:, 0, t:t + 1], None, ALU.mult)
            last.then_inc(crep_done, 1)
            norm_tile(0)
            norm_tile(1)
            weights_lo(0)
            weights_lo(1)
            norm_tile(2)
            norm_tile(3)
            mod_rows_out(0)
            mod_columns(0)
            for t in range(3):
                split_tile(t)
            weights_lo(2)
            split_tile(3)
            weights_lo(3)
            for b in range(QB):
                for m in range(MT):
                    if b == 0 and m + AHEAD < MW:
                        weights_lo(m + AHEAD)
                    qk_out(b * MT + m)
                    nxt = (b + 1) * BT + m // 2
                    if b + 1 < QB and m < 2 * BT:
                        if m % 2 == 0:
                            norm_tile(nxt)
                        else:
                            split_tile(nxt)
                    if mod_place(b, FT - 1) is not None:
                        if m == FT:
                            mod_rows_out(b)
                        if m == FT + 1:
                            mod_columns(b)

        @block.tensor
        def _(pe):
            def modulation(g, k, buf, loaded):
                pe.wait_ge(*loaded)
                for j in range(4):
                    last = nc.tensor.matmul(modp[32 * j:32 * j + 32, :], crep[:, k, :], buf[:, j * NB:(j + 1) * NB],
                                            start=(k == 0), stop=(k == FT - 1))
                last.then_inc(mod_used, 1)

            def modulation_T(g):
                pe.wait_ge(mod_rows, g + 1)
                for k in range(NB // P):
                    ins = nc.tensor.transpose(modp[:, k * P:(k + 1) * P], rows[:, k * P:(k + 1) * P], ident[:])
                ins.then_inc(mod_T, 1)

            def transposes(t):
                pe.wait_ge(xn_done, t + 1)
                if t >= 3:
                    pe.wait_ge(aff_done, 1 if t == 3 else t)
                for f in range(FT):
                    ins = nc.tensor.transpose(transposed(t, f), xt[t % 2][:, f * P:(f + 1) * P], ident[:])
                ins.then_inc(tr_done, 1)

            pe.wait_ge(ident_done, 1)
            pe.wait_ge(crep_done, 1)
            for k in range(FT):
                modulation(0, k, wmod_0[k % NR], (wmod_loaded0[k % NR], 16 * (k // NR + 1)))
                if k in (2, 3, 6):
                    transposes((2, 3, 6).index(k))
            modulation_T(0)
            transposes(3)
            for b in range(QB):
                pe.wait_ge(h_split, BT * (b + 1))
                for m in range(MT):
                    cc = b * MT + m
                    if b == 0:
                        pe.wait_ge(w_split, m + 1)
                    if cc >= QKB:
                        pe.wait_ge(qk_evac, cc - QKB + 1)
                    for k in range(FT):
                        for n, (a, z) in enumerate(TERMS):
                            ins = nc.tensor.matmul(qkp[cc % QKB][:], w[a][:, m, k, :], hT[b % 2][z][:, k, :],
                                                   start=(k == 0 and n == 0), stop=(k == FT - 1 and n == 2))
                    ins.then_inc(qk_acc, 1)
                    if b + 1 < QB and m < 2 * BT and m % 2 == 1:
                        transposes((b + 1) * BT + m // 2)
                    i = mod_place(b, m)
                    if i is not None:
                        if m == 0:
                            pe.wait_ge(mod_done, b)
                        modulation(b, m, wmod_12[i % 2], (wmod_loaded[i % 2], 16 * (i // 2 + 1)))
                    if mod_place(b, FT - 1) is not None and m == FT:
                        modulation_T(b)
                if b == 0:
                    pe.wait_ge(w_split, MW)
                for t in range(BT):
                    tt = b * BT + t
                    if tt >= 2:
                        pe.wait_ge(v_evac, tt - 1)
                    for k in range(FT):
                        for n, (a, z) in enumerate(TERMS):
                            ins = nc.tensor.matmul(vp[tt % 2][:, 0:VW].rearrange("p (m c) -> p m c", c=P),
                                                   hT[b % 2][z][:, k, t * P:(t + 1) * P], w[a][:, MT:MW, k, :],
                                                   start=(k == 0 and n == 0), stop=(k == FT - 1 and n == 2))
                    ins.then_inc(v_acc, 1)


def stage_attention(nc, ctx, q_dram, k_dram, v_dram, y_dram, ident, wo_t, wo_raw, wo_loaded):
    NU = HKV * QB
    SR = 3 * DH
    KT = T // P
    NTURN = GH * (NB // P) * (T // NB)
    NT1 = NTURN + 1
    NSM = 4
    TQ = 4
    NP, NS = 8, 4
    PAIRS, QUADS = KT // 2, KT // 4
    RP = 8
    TSTEP = 14
    DEN_AHEAD, DEN_LATE = (9, 12), (0, 7)
    PER = NTURN // KT
    LEAD = KT - TSTEP + 1
    with ExitStack() as st:
        def sb(name, shape, dt=F32):
            return st.enter_context(nc.sbuf_tensor("att_" + name, shape, dt))

        def pb(name, width=NB):
            return st.enter_context(nc.psum_tensor("att_" + name, [P, width], F32))

        def sem(name):
            return st.enter_context(nc.semaphore("att_" + name))

        ks = [sb(f"k_stack{i}", [SR + 2, T], F32R) for i in range(2)]
        qs = [sb(f"q_stack{i}", [SR + 2, GH, NB], F32R) for i in range(4)]
        vg = [sb(f"v_head{i}", [P, KT, DH]) for i in range(2)]
        pr = [sb(f"exp{i}", [P, GH * NB]) for i in range(NP)]
        ps = [sb(f"exp_pair{i}", [P, GH * NB]) for i in range(NS)]
        last_quad = sb("exp_last_quad", [P, GH * NB])
        ones = sb("ones", [P, DH])
        cmax = [sb(f"chunk_max{i}", [P, NTURN]) for i in range(2)]
        rmax = [sb(f"row_max{i}", [P, GH * NB // P]) for i in range(2)]
        mT = [sb(f"max_T_{n}", [GH * NB // P, P], F32R) for n in ("hi", "lo")]
        ysb = [sb(f"y_raw{i}", [P, NB]) for i in range(2)]
        den = [sb(f"den{i}", [P, NB]) for i in range(2)]
        rden = [sb(f"rden{i}", [P, NB]) for i in range(2)]
        yo = [sb(f"y_out{i}", [P, NB]) for i in range(2)]
        stp = [pb(f"scores_T{i}") for i in range(2)]
        smp = [pb(f"scores{i}") for i in range(NSM)]
        yp, dp = pb("y_acc"), pb("den_acc")

        q_loaded, k_loaded, v_loaded = [sem(f"q_loaded{i}") for i in range(4)], sem("k_loaded"), sem("v_loaded")
        st_ready, exp_done = sem("scoresT_ready"), sem("exp_done")
        sm_ready, sm_done = sem("scores_ready"), sem("scores_consumed")
        mT_hi, mT_done, m_stored = sem("max_T_hi"), sem("max_T_done"), sem("max_rows_stored")
        pv_done, pair_done, den_done = sem("pv_done"), sem("pair_done"), sem("den_done")
        quad_done, last_quad_done = sem("quad_done"), sem("last_quad_done")
        y_copied, den_copied, y_done, y_stored = sem("y_copied"), sem("den_copied"), sem("y_done"), sem("y_stored")
        const_done = sem("consts_done")
        rmax_done, rden_done = sem("row_max_done"), sem("rden_done")
        block = st.enter_context(nc.Block())

        BODY = 2 * QB
        LOOPS = (NU - 1) // BODY

        def turns(k):
            if k + LEAD < KT:
                return 1, range(PER * (k + LEAD), PER * (k + LEAD + 1))
            return 2, range(PER * (k + LEAD - KT), PER * (k + LEAD - KT + 1))

        def units(eng, unit):
            unit(0, 0, 0)
            with eng.Fori(0, LOOPS) as it:
                for j in range(BODY):
                    unit(it * BODY + (1 + j), (1 + j) % BODY, it * (BODY // QB) + (1 + j) // QB)
            for u in range(1 + LOOPS * BODY, NU):
                unit(u, u % BODY, u // QB)

        def is_first(u):
            return isinstance(u, int) and u == 0

        def nth_turn(u, q):
            return q if is_first(u) else u * NT1 + (q if q >= TQ else q - 1)

        def nth_transpose(u):
            return u * NT1 + (NTURN if beyond(u, 1) else NT1 + TQ - 1)

        def turn_buffer(u, c, q):
            return smp[nth_turn(u if is_first(u) else BODY + c, q) % NSM]

        def transpose_buffer(u, c):
            return smp[nth_transpose(u if beyond(u, 1) else c) % NSM][0:GH * NB // P, 0:P]

        def beyond(u, n):
            return isinstance(u, int) and u + n >= NU

        @block.sync
        def _(sp):
            qv = [q_dram[n].rearrange("(h d) t -> d h t", d=DH) for n in range(2)]

            def load_q(c, g):
                for r, n in enumerate((0, 0, 1)):
                    sp.dma_start(qs[c % 4][r * DH:(r + 1) * DH, :, :].bitcast(F32),
                                 qv[n][:, bass.ds(g * GH, GH), c % QB * NB:(c % QB + 1) * NB].bitcast(F32)
                                 ).then_inc(q_loaded[c % 4], 16)

            def load_k(par, g):
                for r, n in enumerate((0, 1, 0)):
                    sp.dma_start(ks[par][r * DH:(r + 1) * DH, :].bitcast(F32),
                                 k_dram[n, bass.ds(g * DH, DH), :].bitcast(F32)).then_inc(k_loaded, 16)

            def load_v(par, g):
                sp.dma_start(vg[par][:], v_dram[:, bass.ds(g * DH, DH)].rearrange("(k p) d -> p k d", p=P)
                             ).then_inc(v_loaded, 16)

            def store_y(u, c, g):
                sp.wait_ge(y_done, 2 + u + 1)
                sp.dma_start(y_dram[bass.ds(g * GH * DH, P), c % QB * NB:(c % QB + 1) * NB], yo[c % 2][:]
                             ).then_inc(y_stored, 16)

            def store_max(u, c):
                sp.wait_ge(sm_done, nth_transpose(u) + 1 + NSM)
                for n in range(2):
                    sp.dma_start(qs[c % 4][SR + n:SR + n + 1, :, :].bitcast(F32), mT[n][:].bitcast(F32)
                                 ).then_inc(m_stored, 16)

            load_k(0, 0)
            for u in range(3):
                load_q(u, u // QB)
            load_v(0, 0)
            for k in range(FT):
                sp.dma_start(wo_raw[:, k, :], wo_t[k]).then_inc(wo_loaded, 16)

            store_max(0, 0)

            def unit(u, c, g):
                if not beyond(u, 3):
                    if not is_first(u):
                        sp.wait_ge(st_ready, u * (GH * KT))
                    load_q((c + 3) % BODY, g + (c % QB + 3) // QB)
                if c % QB == 1 and not beyond(u, 2 * QB - 1 - QB):
                    sp.wait_ge(pv_done, NP + (u - 1) * KT)
                    load_k((c // QB + 1) % 2, g + 1)
                    load_v((c // QB + 1) % 2, g + 1)
                if not beyond(u, 1):
                    store_max(u + 1, c + 1)
                if not is_first(u):
                    store_y(u - 1, (c - 1) % BODY, g if c % QB else g - 1)

            units(sp, unit)
            store_y(NU - 1, (NU - 1) % BODY, HKV - 1)
            sp.wait_ge(y_stored, 16 + 16 * NU)

        @block.gpsimd
        def _(pool):
            def unit(u, c, g):
                for j in range(PAIRS):
                    pool.wait_ge(exp_done, 2 + 2 * GH * (j + 1) + u * (GH * KT))
                    if j in (0, 4, 6):
                        pool.wait_ge(den_done, 1 + j // 2 + u * QUADS)
                    elif j == 2 and not is_first(u):
                        pool.wait_ge(last_quad_done, u)
                    nc.gpsimd.tensor_tensor(ps[j % NS][:], pr[2 * j % NP][:], pr[(2 * j + 1) % NP][:],
                                            ALU.add).then_inc(pair_done, 1)
                    if j % 2 == 1 and j < PAIRS - 1:
                        pool.wait_ge(pair_done, NP // 2 + j + 1 + u * PAIRS)
                        first = ps[(j - 1) % NS]
                        nc.gpsimd.tensor_tensor(first[:], first[:], ps[j % NS][:], ALU.add).then_inc(quad_done, 1)

            pool.sem_inc(pair_done, NP // 2)
            units(pool, unit)

        @block.scalar
        def _(act):
            def copy_y(u, c):
                act.wait_ge(pv_done, NP + KT + u * KT)
                act.wait_ge(y_done, u + 1)
                nc.scalar.copy(ysb[c % 2][:], yp[:]).then_inc(y_copied, 1)

            def copy_den(u, c):
                act.wait_ge(den_done, 2 + QUADS + u * QUADS)
                nc.scalar.copy(den[c % 2][:], dp[:]).then_inc(den_copied, 1)

            def unit(u, c, g):
                for k in range(KT):
                    for h in range(GH):
                        act.wait_ge(st_ready, GH * k + h + 1 + u * (GH * KT))
                        if h == 0:
                            act.wait_ge(pv_done, k + 1 + u * KT)
                            act.wait_ge(pair_done, k // 2 + 1 + u * PAIRS)
                        nc.scalar.activation(pr[k % NP][:, h * NB:(h + 1) * NB], stp[h % 2][:],
                                             ACT.Exp, scale=INV_SQRT_DH).then_inc(exp_done, 1)
                    if k == 0 and not is_first(u):
                        copy_y(u - 1, c - 1)
                    if k == 7 and not is_first(u):
                        copy_den(u - 1, c - 1)

            act.sem_inc(exp_done, 2)
            units(act, unit)
            copy_y(NU - 1, NU - 1)
            copy_den(NU - 1, NU - 1)

        @block.vector
        def _(v):
            def turn(u, c, q):
                v.wait_ge(sm_ready, nth_turn(u, q) + 1)
                nc.vector.reduce_max(cmax[c % 2][:, q:q + 1], turn_buffer(u, c, q)[:], AX.X).then_inc(sm_done, 1)

            def row_max(u, c):
                v.wait_ge(sm_done, nth_turn(u, NTURN - 1) + 1 + NSM)
                nc.vector.reduce_max(rmax[c % 2][:], cmax[c % 2][:].rearrange("p (r k) -> p r k", k=T // NB),
                                     AX.X).then_inc(rmax_done, 1)

            def max_rows(u, c):
                src = transpose_buffer(u, c)
                v.wait_ge(sm_ready, nth_transpose(u) + 1)
                v.wait_ge(m_stored, u * 32)
                nc.vector.tensor_copy(mT[0][:], src).then_inc(mT_hi, 1)
                v.wait_ge(mT_hi, u + 1)
                nc.vector.tensor_tensor(mT[1][:], src, mT[0][:].bitcast(F32), ALU.subtract).then_inc(sm_done, 1)

            def recip(u, c, n):
                cols = slice(n * NB // RP, (n + 1) * NB // RP)
                v.wait_ge(den_copied, u + 1)
                nc.vector.reciprocal(rden[c % 2][:, cols], den[c % 2][:, cols]).then_inc(rden_done, 1)

            def last_quad_part(u, n):
                cols = slice(n * NB, (n + 1) * NB)
                v.wait_ge(pair_done, NP // 2 + PAIRS + u * PAIRS)
                v.wait_ge(den_done, 2 + u * QUADS)
                ins = nc.vector.tensor_tensor(last_quad[:, cols], ps[(PAIRS - 2) % NS][:, cols],
                                              ps[(PAIRS - 1) % NS][:, cols], ALU.add)
                if n == GH - 1:
                    ins.then_inc(last_quad_done, 1)

            def y_out(u, c):
                v.wait_ge(rden_done, RP + u * RP)
                v.wait_ge(y_copied, u + 1)
                v.wait_ge(y_stored, 16 + u * 16)
                nc.vector.tensor_tensor(yo[c % 2][:], ysb[c % 2][:], rden[c % 2][:], ALU.mult).then_inc(y_done, 1)

            def unit(u, c, g):
                for k in range(KT):
                    n, ahead = turns(k)
                    for i, q in enumerate(ahead):
                        if i == 0 and k == TSTEP and not beyond(u, 1):
                            max_rows(u + 1, c + 1)
                        if not beyond(u, n):
                            turn(u + n, c + n, q)
                        if i == 0 and not is_first(u):
                            if 3 <= k < 3 + GH:
                                last_quad_part(u - 1, k - 3)
                            if k >= KT + 1 - RP:
                                recip(u - 1, c - 1, k - (KT + 1 - RP))
                        if i == 2 and k == KT - 1 and not is_first(u):
                            recip(u - 1, c - 1, RP - 1)
                    if k == TSTEP - 2 and not beyond(u, 1):
                        row_max(u + 1, c + 1)
                if not is_first(u):
                    y_out(u - 1, c - 1)

            for i in range(2):
                nc.vector.memset(ks[i][SR:SR + 2, :].bitcast(F32), -1.0)
            nc.vector.memset(ones[:], 1.0).then_inc(const_done, 1)
            v.sem_inc(sm_done, NSM)
            v.sem_inc(y_done, 2)
            v.sem_inc(y_stored, 16)
            for q in range(NTURN):
                turn(0, 0, q)
            row_max(0, 0)
            for q in range(PER * LEAD):
                if q == TQ:
                    max_rows(0, 0)
                turn(1, 1, q)
            units(v, unit)
            for n in range(GH):
                last_quad_part(NU - 1, n)
            for n in range(RP):
                recip(NU - 1, NU - 1, n)
            y_out(NU - 1, NU - 1)

        @block.tensor
        def _(pe):
            def turn(u, c, g, q):
                h, qt, kc = q // 16, q // 4 % 4, q % 4
                if q == 0:
                    pe.wait_ge(q_loaded[c % 4], 48 + g * 48)
                    if c % QB == 0:
                        pe.wait_ge(k_loaded, 48 + g * 48)
                pe.wait_ge(sm_done, nth_turn(u, q) + 1)
                nc.tensor.matmul(turn_buffer(u, c, q)[:], qs[c % 4][0:SR, h, qt * P:(qt + 1) * P],
                                 ks[c // QB % 2][0:SR, kc * NB:(kc + 1) * NB], start=True, stop=True
                                 ).then_inc(sm_ready, 1)

            def transpose_max(u, c):
                pe.wait_ge(sm_done, nth_transpose(u) + 1)
                pe.wait_ge(rmax_done, u + 1)
                nc.tensor.transpose(transpose_buffer(u, c), rmax[c % 2][:], ident[:]
                                    ).then_inc(sm_ready, 1)

            def scores_t(u, c, k, h):
                pe.wait_ge(exp_done, GH * k + h + 1 + u * (GH * KT))
                nc.tensor.matmul(stp[h % 2][:], ks[c // QB % 2][0:SR + 2, k * P:(k + 1) * P],
                                 qs[c % 4][0:SR + 2, h, :], start=True, stop=True).then_inc(st_ready, 1)

            def by_v(u, c, g, k):
                pe.wait_ge(exp_done, 2 + GH * (k + 1) + u * (GH * KT))
                if k == 0:
                    pe.wait_ge(y_copied, u)
                    if c % QB == 0:
                        pe.wait_ge(v_loaded, 16 + g * 16)
                for h in range(GH):
                    ins = nc.tensor.matmul(yp[h * DH:(h + 1) * DH, :], vg[c // QB % 2][:, k, :],
                                           pr[k % NP][:, h * NB:(h + 1) * NB], start=(k == 0), stop=(k == KT - 1))
                ins.then_inc(pv_done, 1)

            def denominators(u, i):
                if i < QUADS - 1:
                    pe.wait_ge(quad_done, i + 1 + u * (QUADS - 1))
                    quad = ps[2 * i % NS]
                else:
                    pe.wait_ge(last_quad_done, u + 1)
                    quad = last_quad
                if i == 0:
                    pe.wait_ge(den_copied, u)
                for h in range(GH):
                    ins = nc.tensor.matmul(dp[h * DH:(h + 1) * DH, :], ones[:], quad[:, h * NB:(h + 1) * NB],
                                           start=(i == 0), stop=(i == QUADS - 1))
                ins.then_inc(den_done, 1)

            def unit(u, c, g):
                for k in range(KT):
                    n, ahead = turns(k)
                    ahead = [] if beyond(u, n) else list(ahead)

                    def ahead_turn():
                        for q in ahead[:1]:
                            turn(u + n, (c + n) % BODY, g + (c % QB + n) // QB, q)
                        del ahead[:1]

                    if k == 0:
                        pe.wait_ge(m_stored, 32 + u * 32)
                    scores_t(u, c, k, 0)
                    if k == TSTEP and not beyond(u, 1):
                        transpose_max(u + 1, (c + 1) % BODY)
                    ahead_turn()
                    scores_t(u, c, k, 1)
                    if k > 0:
                        by_v(u, c, g, k - 1)
                    elif not is_first(u):
                        by_v(u - 1, (c - 1) % BODY, g, KT - 1)
                    scores_t(u, c, k, 2)
                    ahead_turn()
                    scores_t(u, c, k, 3)
                    ahead_turn()
                    ahead_turn()
                    if k in DEN_AHEAD:
                        denominators(u, DEN_AHEAD.index(k))
                    if k in DEN_LATE and not is_first(u):
                        denominators(u - 1, 2 + DEN_LATE.index(k))

            pe.sem_inc(pv_done, NP)
            pe.sem_inc(den_done, 2)
            pe.wait_ge(const_done, 1)
            for q in range(NTURN):
                turn(0, 0, 0, q)
            for q in range(PER * LEAD):
                if q == TQ:
                    transpose_max(0, 0)
                turn(1, 1, 0, q)
            units(pe, unit)
            by_v(NU - 1, (NU - 1) % BODY, HKV - 1, KT - 1)
            for i in (QUADS - 2, QUADS - 1):
                denominators(NU - 1, i)


def stage_out_projection(nc, ctx, x, y_dram, bo, mod_dram, x1_dram, wo_raw, h2_hi, h2lo_dram, modT, ident,
                         wo_loaded, wg_t, wu_t, shared, h2_lo0, gu_loaded, lo0_loaded):
    with ExitStack() as st:
        def sb(name, shape, dt=F32):
            return st.enter_context(nc.sbuf_tensor("wo_" + name, shape, dt))

        def pb(name, width=2 * NB):
            return st.enter_context(nc.psum_tensor("wo_" + name, [P, width], F32))

        def sem(name):
            return st.enter_context(nc.semaphore("wo_" + name))

        w = [sb(f"wo_{n}", [P, FT, D], F32R) for n in ("hi", "lo")]
        yraw, y2, y4 = ([shared[n][:, i * HALF_W:(i + 1) * HALF_W].rearrange("p (k t) -> p k t", t=P) for i in (j, j + 1)]
                        for n, j in ((0, 0), (1, 2), (1, 4)))
        ysp = [y2, y4]
        xt = [sb(f"x1_tile{i}", [P, D]) for i in range(2)]
        xn = sb("x1_norm", [P, D])
        work = sb("gated", [P, D])
        gate, bias = sb("gate_a", [P, D]), sb("bo_rows", [P, D])
        stats, mv, s = sb("ln2_stats", [P, 12]), sb("ln2_mv", [P, 2]), sb("ln2_s", [P, 8])
        aff = sb("h2_affine", [P, FT, P])
        lo = [sb(f"h2_lo{i}", [P, FT, P], F32R) for i in range(2)]
        acc = [pb(f"wo_acc{i}") for i in range(2)]
        tr = pb("h2_T")

        w_hi, w_split = sem("wo_hi"), sem("wo_split")
        g_loaded, y_loaded, x_loaded = (
            sem("gate_loaded"), [sem(f"y_loaded{i}") for i in range(2)], [sem(f"x_loaded{i}") for i in range(2)])
        y_hi, y_split, acc_done, x1_done, x1_stored = (
            sem("y_hi"), sem("y_split"), sem("acc_done"), sem("x1_done"), sem("x1_stored"))
        var_done, root_done, xn_done, tr_done, aff_done = (
            sem("var_done"), sem("root_done"), sem("xn_done"), sem("tr_done"), sem("aff_done"))
        h_hi, h_split, lo_stored, dve = sem("h2_hi"), sem("h2_split"), sem("h2lo_stored"), sem("out_dve_links")
        stats_seen = sem("stats_seen")
        x_view = x.rearrange("a (t p) d -> (a t) p d", p=P)
        x1_view = x1_dram.rearrange("(t p) d -> t p d", p=P)
        y_view = y_dram.rearrange("(k p) t -> p k t", p=P)
        POST_LINKS = 2 + 3 + 5

        block = st.enter_context(nc.Block())

        MID = TT - 2
        BT = NB // P

        def tiles(eng, tile):
            for t in range(2):
                tile(t, t, 0, t)
            with eng.Fori(0, (MID - 2) // 2) as i:
                for j in range(2):
                    tile(i * 2 + (2 + j), j, i + 1, None)
            for t in range(MID, TT):
                tile(t, t % 2, t // 2, t)

        @block.sync
        def _(sp):
            def load_y(t, j):
                sp.dma_start(yraw[j], y_view[:, :, bass.ds(t * P, P)]).then_inc(y_loaded[j], 16)

            def load_x(t, j):
                sp.dma_start(xt[j][:], x_view[t]).then_inc(x_loaded[j], 16)

            load_y(0, 0)
            load_y(1, 1)
            load_x(0, 0)
            load_x(1, 1)

            def tile(t, j, h, known):
                if known is None or known + 2 < TT:
                    sp.wait_ge(y_split, t + 1)
                    load_y(t + 2, j)
                sp.wait_ge(x1_done, t + 1)
                sp.dma_start(x1_view[t], xt[j][:]).then_inc(x1_stored, 16)
                if known is None or known + 2 < TT:
                    sp.wait_ge(x1_stored, t * 16 + 16)
                    sp.wait_ge(xn_done, t + 1)
                    load_x(t + 2, j)

                if known == MID:
                    sp.wait_ge(lo_stored, 16 * BT)
                    for b in range(BT):
                        sp.dma_start(h2_lo0[:, :, b * P:(b + 1) * P].bitcast(F32), h2lo_dram[b].bitcast(F32)
                                     ).then_inc(lo0_loaded, 16)
                    sp.wait_ge(y_split, TT)
                    load_gate_up(sp, shared[0], wg_t, wu_t, 0, gu_loaded)

            tiles(sp, tile)
            sp.wait_ge(x1_stored, 16 * TT)

        @block.gpsimd
        def _(pool):
            pool.dma_start(gate[:], mod_dram[2 * D:3 * D].rearrange("(a d) -> a d", a=1).broadcast_to([P, D])
                           ).then_inc(g_loaded, 16)
            pool.dma_start(bias[:], bo.rearrange("(a d) -> a d", a=1).broadcast_to([P, D])).then_inc(g_loaded, 16)
            def tile(t, j, h, known):
                pool.wait_ge(h_split, t + 1)
                pool.dma_start(h2lo_dram[t].bitcast(F32), lo[j][:].bitcast(F32)).then_inc(lo_stored, 16)

            tiles(pool, tile)
            pool.wait_ge(lo_stored, 16 * TT)

        @block.scalar
        def _(act):
            def hi_of_y(t, j, h):
                act.wait_ge(y_loaded[j], h * 16 + 16)
                nc.scalar.copy(ysp[j][0], yraw[j]).then_inc(y_hi, 1)

            act.wait_ge(wo_loaded, 16 * FT)
            for k in range(FT):
                nc.scalar.copy(w[0][:, k, :], wo_raw[:, k, :]).then_inc(w_hi, 1)
                if k == 0:
                    hi_of_y(0, 0, 0)
            hi_of_y(1, 1, 0)

            def tile(t, j, h, known):
                act.wait_ge(var_done, t + 1)
                nc.scalar.activation(s[:, 1:2], s[:, 0:1], ACT.Sqrt).then_inc(root_done, 1)
                if known is None or known + 2 < TT:
                    act.wait_ge(acc_done, t + 1)
                    hi_of_y(t + 2, j, h + 1)
                act.wait_ge(tr_done, t + 1)
                act.wait_ge(h_split, t)
                for f in range(FT):
                    ins = nc.scalar.activation(aff[:, f, :], tr[:, f * P:(f + 1) * P], ACT.Identity,
                                               scale=modT[:, 32 + f:33 + f], bias=modT[:, 24 + f:25 + f])
                ins.then_inc(aff_done, 1)

            tiles(act, tile)

        @block.vector
        def _(v):
            ln = Links(v, dve)

            def lo_of_y(t, j):
                v.wait_ge(y_hi, t + 1)
                nc.vector.tensor_tensor(ysp[j][1], yraw[j], ysp[j][0].bitcast(F32),
                                        ALU.subtract).then_inc(y_split, 1)

            for k in range(FT):
                v.wait_ge(w_hi, k + 1)
                nc.vector.tensor_tensor(w[1][:, k, :], wo_raw[:, k, :], w[0][:, k, :].bitcast(F32),
                                        ALU.subtract).then_inc(w_split, 1)
                if k == 0:
                    lo_of_y(0, 0)
            lo_of_y(1, 1)
            v.wait_ge(g_loaded, 32)
            gate_of(nc, ln, gate, work)

            setup = ln.n

            def split(t, j):
                v.wait_ge(aff_done, t + 1)
                v.wait_ge(lo_stored, t * 16)
                for half in range(2):
                    fs = slice(half * FT // 2, (half + 1) * FT // 2)
                    hi = h2_hi[half][:, :, bass.ds(t * P, P)]
                    nc.vector.tensor_copy(hi, aff[:, fs]).then_inc(h_hi, 1)
                    v.wait_ge(h_hi, t * 2 + (half + 1))
                    ins = nc.vector.tensor_tensor(lo[j][:, fs], aff[:, fs], hi.bitcast(F32), ALU.subtract)
                ins.then_inc(h_split, 1)

            def tile(t, j, h, known):
                ln.base, ln.n = t * POST_LINKS + setup, 0
                v.wait_ge(acc_done, t + 1)
                v.wait_ge(x_loaded[j], h * 16 + 16)
                ln.link(nc.vector.tensor_tensor(work[:], acc[j][:], bias[:], ALU.add))
                ln.link(nc.vector.tensor_tensor(work[:], work[:], gate[:], ALU.mult))
                nc.vector.tensor_tensor(xt[j][:], xt[j][:], work[:], ALU.add).then_inc(x1_done, 1)
                v.wait_ge(x1_done, t + 1)
                ln.link(nc.vector.bn_stats(stats[:, 0:6], xt[j][:, 0:NB]))
                ln.link(nc.vector.bn_stats(stats[:, 6:12], xt[j][:, NB:D]))
                v.sem_inc(stats_seen, 1)
                ln.link(nc.vector.bn_aggr(mv[:], stats[:]))
                rsqrt_steps(nc, v, ln, mv, s, var_done, root_done, t + 1)
                v.wait_ge(tr_done, t)
                nc.vector.tensor_scalar(xn[:], xt[j][:], mv[:, 0:1], s[:, 4:5],
                                        ALU.subtract, ALU.mult).then_inc(xn_done, 1)
                if known is None or known + 2 < TT:
                    lo_of_y(t + 2, j)
                if known != 0:
                    split(t - 1, 1 - j)

            tiles(v, tile)
            split(TT - 1, (TT - 1) % 2)

        @block.tensor
        def _(pe):
            def project(t, j):
                pe.wait_ge(y_split, t + 1)
                for half in range(2):
                    for k in range(FT):
                        if half == 0 and isinstance(t, int) and t == 0:
                            pe.wait_ge(w_split, k + 1)
                        for n, (a, z) in enumerate(TERMS):
                            ins = nc.tensor.matmul(acc[j][:, half * NB:(half + 1) * NB], ysp[j][a][:, k, :],
                                                   w[z][:, k, half * NB:(half + 1) * NB],
                                                   start=(k == 0 and n == 0), stop=(k == FT - 1 and n == 2))
                ins.then_inc(acc_done, 1)

            def tile(t, j, h, known):
                if known is None or known + 1 < TT:
                    if known != 0:
                        pe.wait_ge(x1_done, t)
                    project(t + 1, 1 - j)
                pe.wait_ge(xn_done, t + 1)
                pe.wait_ge(aff_done, t)
                for f in range(FT):
                    ins = nc.tensor.transpose(tr[:, f * P:(f + 1) * P], xn[:, f * P:(f + 1) * P], ident[:])
                ins.then_inc(tr_done, 1)

            project(0, 0)
            tiles(pe, tile)


def gate_of(nc, ln, gate, work):
    ln.link(nc.vector.tensor_scalar(work[:], gate[:], -1.0, 0.25, ALU.mult, ALU.max))
    ln.link(nc.vector.tensor_tensor(work[:], work[:], gate[:], ALU.max))
    ln.link(nc.vector.tensor_scalar(gate[:], gate[:], 0.0, 2.0, ALU.is_ge, ALU.mult))
    ln.link(nc.vector.tensor_scalar_add(gate[:], gate[:], -1.0))
    ln.link(nc.vector.tensor_tensor(gate[:], gate[:], work[:], ALU.mult))


def trunc_tail(nc, v, ln, out, rnd, mag, sgn, tmp):
    ln.link(nc.vector.tensor_tensor(tmp, rnd, mag, ALU.is_gt))
    ln.link(nc.vector.tensor_tensor(rnd, rnd, tmp, ALU.subtract))
    return nc.vector.tensor_tensor(out, rnd, sgn, ALU.mult)


def load_gate_up(sp, raw, wg_t, wu_t, first, loaded):
    for n, wt in enumerate((wg_t, wu_t)):
        sp.dma_start(raw[:, n * HALF_W:(n + 1) * HALF_W].rearrange("p (k c) -> p k c", c=P),
                     wt.rearrange("(k p) n -> p k n", p=P)[:, :, bass.ds(first, P)]).then_inc(loaded, 16)


def stage_gate_up(nc, ctx, wg_t, wu_t, h2_hi, h2_lo0, h2lo_dram, inter_dram, shared,
                  gu_loaded, lo0_loaded, wd_t, down_loaded):
    with ExitStack() as st:
        def sb(name, shape, dt=F32):
            return st.enter_context(nc.sbuf_tensor("gu_" + name, shape, dt))

        def pb(name):
            return st.enter_context(nc.psum_tensor("gu_" + name, [P, NB], F32))

        def sem(name):
            return st.enter_context(nc.semaphore("gu_" + name))

        h2_lo = [h2_lo0] + [sb(f"h2_lo{b}", [P, FT, NB], F32R) for b in range(1, QB)]
        wraw = [shared[0], sb("w_raw1", [P, 2 * HALF_W])]
        w = [[shared[1][:, n * 2 * HALF_W:(n + 1) * 2 * HALF_W] for n in (1, 2)],
             [sb(f"w_{n}1", [P, 2 * HALF_W], F32R) for n in ("hi", "lo")]]
        sig = sb("sigmoid", [P, NB])
        val, mag, sgn, rnd = sb("value", [P, NB]), sb("magnitude", [P, NB]), sb("sign", [P, NB]), sb("rounded", [P, NB])
        out = [sb(f"inter{i}", [P, NB], I8) for i in range(2)]
        gp, up = [pb(f"gate_acc{i}") for i in range(2)], [pb(f"up_acc{i}") for i in range(2)]

        h_loaded = [lo0_loaded] + [sem(f"h2lo_loaded{b}") for b in range(1, QB)]
        w_loaded, w_hi, w_split = [gu_loaded, sem("w_loaded1")], sem("w_hi"), sem("w_split")
        g_acc, u_acc, sig_done, val_done, parts_done, out_done, out_stored = (
            sem("gate_acc_done"), sem("up_acc_done"), sem("sigmoid_done"), sem("value_done"), sem("abs_sign_done"),
            sem("inter_done"), sem("inter_stored"))
        gate_split, last_stored = sem("gate_w_split"), sem("last_inter_stored")
        dve = sem("gu_dve_links")
        LINKS = 5
        block = st.enter_context(nc.Block())

        def tiles(eng, tile):
            with eng.Fori(0, (IT - 2) // 2) as it:
                for j in range(2):
                    tile(it * 2 + j, j, it, False)
            for i in range(IT - 2, IT):
                tile(i, i % 2, i // 2, i == IT - 1)

        def store_inter(eng, i, last):
            rows = slice(P - LASTI, P) if last else slice(0, P)
            for n in range(QB):
                eng.wait_ge(out_done, n + 2 + i * QB)
                eng.dma_start(inter_dram[i, 0:LASTI if last else P, n * NB:(n + 1) * NB], out[n % 2][rows, :]
                              ).then_inc(last_stored if last else out_stored, 16)

        @block.sync
        def _(sp):
            def load_w(i, j):
                first = INTER - P if isinstance(i, int) and i == IT - 1 else i * P
                load_gate_up(sp, wraw[j], wg_t, wu_t, first, w_loaded[j])

            for b in range(1, QB):
                for t in range(TT // QB):
                    sp.dma_start(h2_lo[b][:, :, t * P:(t + 1) * P].bitcast(F32),
                                 h2lo_dram[b * (TT // QB) + t].bitcast(F32)).then_inc(h_loaded[b], 16)
                if b == 1:
                    load_w(1, 1)
            with sp.Fori(0, (IT - 4) // 2) as it:
                for j in range(2):
                    sp.wait_ge(w_split, it * 2 + (j + 1))
                    load_w(it * 2 + (j + 2), j)
            for i in range(IT - 2, IT):
                sp.wait_ge(w_split, i - 1)
                load_w(i, i % 2)
            sp.wait_ge(u_acc, 1 + QB * (IT - 1))
            load_down(sp, shared[0], wd_t, 0, down_loaded)
            store_inter(sp, IT - 1, True)
            sp.wait_ge(last_stored, 16 * QB)

        @block.gpsimd
        def _(pool):
            def tile(i, j, h, last):
                if not last:
                    store_inter(pool, i, False)

            tiles(pool, tile)
            pool.wait_ge(out_stored, 16 * QB * (IT - 1))

        @block.scalar
        def _(act):
            def weights_hi(j, h):
                act.wait_ge(w_loaded[j], h * 32 + 32)
                for n in range(2):
                    cols = slice(n * HALF_W, (n + 1) * HALF_W)
                    nc.scalar.copy(w[j][0][:, cols], wraw[j][:, cols]).then_inc(w_hi, 1)

            def tile(i, j, h, last):
                for n in range(QB):
                    act.wait_ge(g_acc, n + 1 + i * QB)
                    act.wait_ge(val_done, n + 2 + i * QB)
                    nc.scalar.activation(sig[:], gp[n % 2][:], ACT.Sigmoid, scale=1.0 / 128.0).then_inc(sig_done, 1)
                    act.wait_ge(val_done, n + 3 + i * QB)
                    nc.scalar.activation(mag[:], val[:], ACT.Abs)
                    nc.scalar.activation(sgn[:], val[:], ACT.Sign).then_inc(parts_done, 1)
                    if n == 1 and not last:
                        act.wait_ge(u_acc, 1 + i * QB)
                        weights_hi(1 - j, h + j)

            weights_hi(0, 0)
            tiles(act, tile)

        @block.vector
        def _(v):
            ln = Links(v, dve)

            def weights_lo(i, j):
                for n in range(2):
                    cols = slice(n * HALF_W, (n + 1) * HALF_W)
                    v.wait_ge(w_hi, i * 2 + (n + 1))
                    ins = nc.vector.tensor_tensor(w[j][1][:, cols], wraw[j][:, cols], w[j][0][:, cols].bitcast(F32),
                                                  ALU.subtract)
                    ins.then_inc(gate_split if n == 0 else w_split, 1)

            def tile(i, j, h, last):
                for n in range(QB):
                    ln.base, ln.n = i * (QB * LINKS) + n * LINKS, 0
                    v.wait_ge(sig_done, n + 1 + i * QB)
                    v.wait_ge(out_done, n + 1 + i * QB)
                    ln.link(nc.vector.scalar_tensor_tensor(out=rnd[:], in0=gp[n % 2][:], scalar=1.0 / 128.0,
                                                           in1=sig[:], op0=ALU.mult, op1=ALU.mult))
                    v.wait_ge(u_acc, n + 2 + i * QB)
                    ln.link(nc.vector.tensor_tensor(rnd[:], up[n % 2][:], rnd[:], ALU.mult))
                    nc.vector.tensor_scalar(val[:], rnd[:], 127.0, -128.0, ALU.min, ALU.max).then_inc(val_done, 1)
                    v.wait_ge(parts_done, n + 1 + i * QB)
                    ln.link(nc.vector.tensor_scalar(rnd[:], mag[:], RNE, -RNE, ALU.add, ALU.add))
                    if n == 1 and last:
                        v.wait_ge(out_stored, 16 * QB * (IT - 1))
                    if n and last:
                        v.wait_ge(last_stored, n * 16)
                    elif n:
                        v.wait_ge(out_stored, n * 16 + i * (QB * 16))
                    trunc_tail(nc, v, ln, out[n % 2][:], rnd[:], mag[:], sgn[:], val[:]).then_inc(out_done, 1)
                    if n == 1 and not last:
                        weights_lo(i + 1, 1 - j)

            v.sem_inc(val_done, 2)
            v.sem_inc(out_done, 1)
            v.sem_inc(u_acc, 1)
            weights_lo(0, 0)
            tiles(v, tile)

        @block.tensor
        def _(pe):
            def tile(i, j, h, last):
                pe.wait_ge(gate_split, i + 1)
                for n in range(QB):
                    pe.wait_ge(val_done, n + 1 + i * QB)
                    pe.wait_ge(h_loaded[n], 16 * TT // QB)
                    for m, (bank, done) in enumerate(((gp, g_acc), (up, u_acc))):
                        if m == 1 and n == 0:
                            pe.wait_ge(w_split, i + 1)
                        for k in range(FT):
                            h2 = h2_hi[k * 2 // FT][:, k % (FT // 2), n * NB:(n + 1) * NB], h2_lo[n][:, k, :]
                            for q, (a, z) in enumerate(TERMS):
                                ins = nc.tensor.matmul(bank[n % 2][:], w[j][a][:, m * HALF_W + k * P:m * HALF_W + (k + 1) * P],
                                                       h2[z],
                                                       start=(k == 0 and q == 0), stop=(k == FT - 1 and q == 2))
                        ins.then_inc(done, 1)

            tiles(pe, tile)


def load_down(sp, raw, wd_t, q, loaded):
    raw = raw[:, 0:IT * QW].rearrange("p (k n) -> p k n", n=QW)
    cols = slice(q * QW, (q + 1) * QW)
    sp.dma_start(raw[:, 0:IT - 1, :], wd_t[0:(IT - 1) * P, cols].rearrange("(k p) n -> p k n", p=P)).then_inc(loaded, 16)
    sp.dma_start(raw[0:LASTI, IT - 1, :], wd_t[(IT - 1) * P:INTER, cols]).then_inc(loaded, 16)


def stage_down(nc, ctx, wd_t, mod_dram, x1_dram, inter_dram, out, shared_raw, lhs_room, down_loaded):
    NQ = D // QW
    with ExitStack() as st:
        def sb(name, shape, dt=F32):
            return st.enter_context(nc.sbuf_tensor("dn_" + name, shape, dt))

        def sem(name):
            return st.enter_context(nc.semaphore("dn_" + name))

        inter = sb("inter_all", [P, IT, T], I8)
        wraw = shared_raw[:, 0:IT * QW].rearrange("p (k n) -> p k n", n=QW)
        w = [[sb(f"wd_{n}{i}", [P, IT, QW], F32R) for n in ("hi", "lo")] for i in range(2)]
        room = lhs_room[:].rearrange("p k t -> p (k t)")
        lhs = [room[:, i * IT * P:(i + 1) * IT * P].rearrange("p (k t) -> p k t", t=P) for i in range(2)]
        gate = sb("gate_b", [P, D])
        gwork = sb("gate_work", [P, D])
        x1t = [sb(f"x1_part{i}", [P, QW]) for i in range(2)]
        ot = [sb(f"out_part{i}", [P, QW]) for i in range(2)]
        raw, val, mag, sgn, rnd = (sb(n, [P, QW]) for n in ("down", "value", "magnitude", "sign", "rounded"))
        acc = [st.enter_context(nc.psum_tensor(f"down_acc{i}", [P, NB], F32)) for i in range(2)]

        i_loaded, w_loaded, w_hi, w_split, g_loaded = (
            [sem(f"inter_loaded{b}") for b in range(QB)], down_loaded, sem("wd_hi"), sem("wd_split"), sem("gateb_loaded"))
        lhs_done, acc_done, raw_done, val_done, parts_done, o_done, o_stored, x_loaded = (
            sem("inter_tile_done"), sem("down_acc_done"), sem("down_copied"), sem("down_clipped"), sem("down_abs_sign"),
            sem("out_done"), sem("out_stored"), [sem(f"x1_loaded{i}") for i in range(2)])
        early_loaded, early_done = sem("early_inter_loaded"), sem("early_inter_tiles_done")
        dve = sem("down_dve_links")
        LINKS = 5
        full = slice(0, IT - 1)
        PARTS = [(slice(0, P), slice(k, min(k + 4, IT - 1))) for k in range(0, IT - 1, 4)]
        EARLY, LATE = slice(0, IT // 2), slice(IT // 2, IT - 1)
        PARTS.append((slice(0, LASTI), slice(IT - 1, IT)))
        block = st.enter_context(nc.Block())

        def steps(eng, step, before=None):
            for q in range(NQ):
                if before:
                    before(q)
                first = 2 if q == 0 else 0
                for t in range(first):
                    step(t, t, t, 0, q)
                with eng.Fori(0, (TT - 2 - first) // 2) as i:
                    for j in range(2):
                        step(i * 2 + (q * TT + j + first), i * 2 + (j + first), j, i + (q * TT + first) // 2, q)
                for t in range(TT - 2, TT):
                    step(q * TT + t, t, t % 2, (q * TT + t) // 2, q)

        @block.sync
        def _(sp):
            for b in range(QB):
                cols = slice(b * NB, (b + 1) * NB)
                if b == 0:
                    sp.dma_start(inter[:, EARLY, cols], inter_dram[EARLY, :, cols].rearrange("k p t -> p k t")
                                 ).then_inc(early_loaded, 16)
                rest = LATE if b == 0 else full
                sp.dma_start(inter[:, rest, cols], inter_dram[rest, :, cols].rearrange("k p t -> p k t")
                             ).then_inc(i_loaded[b], 16)
                sp.dma_start(inter[0:LASTI, IT - 1, cols], inter_dram[IT - 1, 0:LASTI, cols]).then_inc(i_loaded[b], 16)

            def before(q):
                if q + 1 < NQ:
                    sp.wait_ge(w_split, len(PARTS) + q)
                    load_down(sp, shared_raw, wd_t, q + 1, w_loaded)

            def load_x1(t, j, q):
                sp.dma_start(x1t[j][:], x1_dram[bass.ds(t * P, P), q * QW:(q + 1) * QW]).then_inc(x_loaded[j], 16)

            load_x1(0, 0, 0)
            load_x1(1, 1, 0)

            def step(s, t, j, h, q):
                sp.wait_ge(o_done, s + 2)
                sp.dma_start(out[0, bass.ds(t * P, P), q * QW:(q + 1) * QW], ot[j][:]).then_inc(o_stored, 16)
                if not isinstance(t, int) or t + 2 < TT:
                    load_x1(t + 2, j, q)
                elif q + 1 < NQ:
                    load_x1(t + 2 - TT, j, q + 1)

            steps(sp, step, before)
            sp.wait_ge(o_stored, 16 + 16 * NQ * TT)

        @block.gpsimd
        def _(pool):
            pool.dma_start(gate[:], mod_dram[5 * D:6 * D].rearrange("(a d) -> a d", a=1).broadcast_to([P, D])
                           ).then_inc(g_loaded, 16)
            for q in range(1, NQ):
                pool.wait_ge(w_loaded, 32 * (q + 1))
                if q >= 2:
                    pool.wait_ge(acc_done, 2 + TT * (q - 1))
                for rows, ks in ((slice(0, P), full), (slice(0, LASTI), slice(IT - 1, IT))):
                    ins = nc.gpsimd.tensor_copy(w[q % 2][0][rows, ks], wraw[rows, ks])
                ins.then_inc(w_hi, 1)
                pool.wait_ge(w_hi, len(PARTS) + q)
                for rows, ks in ((slice(0, P), full), (slice(0, LASTI), slice(IT - 1, IT))):
                    ins = nc.gpsimd.tensor_tensor(w[q % 2][1][rows, ks], wraw[rows, ks],
                                                  w[q % 2][0][rows, ks].bitcast(F32), ALU.subtract)
                ins.then_inc(w_split, 1)

        @block.scalar
        def _(act):
            def tile_of_inter(s, t, j):
                act.wait_ge(acc_done, s + 1)
                nc.scalar.copy(lhs[j][:, full, :], inter[:, full, bass.ds(t * P, P)])
                nc.scalar.copy(lhs[j][0:LASTI, IT - 1, :], inter[0:LASTI, IT - 1, bass.ds(t * P, P)]).then_inc(lhs_done, 1)

            def step(s, t, j, h, q):
                if not isinstance(t, int) or t + 1 < TT:
                    tile_of_inter(s + 1, t + 1, 1 - j)
                elif q + 1 < NQ:
                    tile_of_inter(s + 1, 0, 1 - j)
                if isinstance(s, int) and s == 1:
                    for b in range(1, QB):
                        act.wait_ge(i_loaded[b], 32)
                act.wait_ge(acc_done, s + 3)
                act.wait_ge(val_done, s + 1)
                nc.scalar.mul(raw[:], acc[j][:, 0:QW], 128.0).then_inc(raw_done, 1)
                act.wait_ge(val_done, s + 2)
                nc.scalar.activation(mag[:], val[:], ACT.Abs)
                nc.scalar.activation(sgn[:], val[:], ACT.Sign).then_inc(parts_done, 1)

            act.wait_ge(w_loaded, 32)
            for n, (rows, ks) in enumerate(PARTS):
                nc.scalar.copy(w[0][0][rows, ks], wraw[rows, ks]).then_inc(w_hi, 1)
                if n == 2:
                    act.wait_ge(early_loaded, 16)
                    nc.scalar.copy(lhs[0][:, EARLY, :], inter[:, EARLY, 0:P]).then_inc(early_done, 1)
                if n == 3:
                    act.wait_ge(i_loaded[0], 32)
                    nc.scalar.copy(lhs[0][:, LATE, :], inter[:, LATE, 0:P])
                    nc.scalar.copy(lhs[0][0:LASTI, IT - 1, :], inter[0:LASTI, IT - 1, 0:P]).then_inc(lhs_done, 1)
            steps(act, step)

        @block.vector
        def _(v):
            ln = Links(v, dve)
            v.sem_inc(acc_done, 2)
            v.sem_inc(raw_done, 2)
            v.sem_inc(val_done, 1)
            v.sem_inc(o_done, 1)
            v.sem_inc(o_stored, 16)
            for n, (rows, ks) in enumerate(PARTS):
                v.wait_ge(w_hi, n + 1)
                nc.vector.tensor_tensor(w[0][1][rows, ks], wraw[rows, ks], w[0][0][rows, ks].bitcast(F32),
                                        ALU.subtract).then_inc(w_split, 1)
            v.wait_ge(g_loaded, 16)
            gate_of(nc, ln, gate, gwork)
            setup = ln.n

            def step(s, t, j, h, q):
                ln.base, ln.n = s * LINKS + setup, 0
                v.wait_ge(raw_done, s + 3)
                nc.vector.tensor_scalar(val[:], raw[:], 127.0, -128.0, ALU.min, ALU.max).then_inc(val_done, 1)
                v.wait_ge(parts_done, s + 1)
                v.wait_ge(o_done, s + 1)
                ln.link(nc.vector.tensor_scalar(rnd[:], mag[:], RNE, -RNE, ALU.add, ALU.add))
                ln.link(trunc_tail(nc, v, ln, rnd[:], rnd[:], mag[:], sgn[:], val[:]))
                ln.link(nc.vector.tensor_tensor(rnd[:], rnd[:], gate[:, q * QW:(q + 1) * QW], ALU.mult))
                v.wait_ge(x_loaded[j], h * 16 + 16)
                v.wait_ge(o_stored, s * 16 + 16)
                nc.vector.tensor_tensor(ot[j][:], x1t[j][:], rnd[:], ALU.add).then_inc(o_done, 1)

            steps(v, step)

        @block.tensor
        def _(pe):
            def step(s, t, j, h, q):
                first = isinstance(s, int) and s == 0
                if first:
                    pe.wait_ge(early_done, 1)
                else:
                    pe.wait_ge(lhs_done, s + 1)
                pe.wait_ge(raw_done, s + 1)
                for k in range(IT):
                    if first and k == EARLY.stop:
                        pe.wait_ge(lhs_done, 1)
                    if isinstance(s, int) and s == 0:
                        part = k // 4 if k < IT - 1 else len(PARTS) - 1
                        pe.wait_ge(w_split, part + 1)
                    rows = slice(0, LASTI if k == IT - 1 else P)
                    for n in range(2):
                        ins = nc.tensor.matmul(acc[j][:, 0:QW], lhs[j][rows, k, :], w[q % 2][n][rows, k, :],
                                               start=(k == 0 and n == 0), stop=(k == IT - 1 and n == 1))
                ins.then_inc(acc_done, 1)

            steps(pe, step, before=lambda q: q and pe.wait_ge(w_split, len(PARTS) + q))


def build(nc, x, wq_t, wk_t, wv_t, wo_t, bo, wg_t, wu_t, wd_t, c, wmod, out):
    mod_dram = nc.dram_tensor("mod_scratch", [6 * D], F32).ap()
    q_dram = nc.dram_tensor("q_scratch", [2, HQ * DH, T], F32).ap()
    k_dram = nc.dram_tensor("k_scratch", [2, HKV * DH, T], F32).ap()
    v_dram = nc.dram_tensor("v_scratch", [T, HKV * DH], F32).ap()
    y_dram = nc.dram_tensor("y_scratch", [HQ * DH, T], F32).ap()
    x1_dram = nc.dram_tensor("x1_scratch", [T, D], F32).ap()
    h2lo_dram = nc.dram_tensor("h2lo_scratch", [TT, P, FT, P], F32).ap()
    inter_dram = nc.dram_tensor("inter_scratch", [IT, P, T], I8).ap()
    with ExitStack() as ctx:
        modT = ctx.enter_context(nc.sbuf_tensor("mod_cols", [P, 48], F32))
        ident = ctx.enter_context(nc.sbuf_tensor("ident", [P, P], F32))
        stage_modulation_and_qkv(nc, ctx, c, wmod, x, wq_t, wk_t, wv_t, mod_dram, q_dram, k_dram, v_dram, modT, ident)
        wo_raw, h2_hi0 = overlay(nc, ctx, ("wo_raw", [P, FT, D], F32), ("h2_hi0", [P, FT // 2, T], F32R))
        wo_loaded = ctx.enter_context(nc.semaphore("wo_preloads"))
        stage_attention(nc, ctx, q_dram, k_dram, v_dram, y_dram, ident, wo_t, wo_raw, wo_loaded)
        shared = overlay(nc, ctx, ("shared_raw", [P, SHARED], F32), ("shared_split", [P, SHARED], F32R))
        gu_loaded = ctx.enter_context(nc.semaphore("gate_up_w_preloads"))
        lo0_loaded = ctx.enter_context(nc.semaphore("h2lo_preloads"))
        down_loaded = ctx.enter_context(nc.semaphore("down_preloads"))
        with nc.sbuf_tensor("h2_hi1", [P, FT // 2, T], F32R) as h2_hi1, nc.sbuf_tensor("h2_lo0", [P, FT, NB], F32R) as h2_lo0:
            h2_hi = [h2_hi0, h2_hi1]
            stage_out_projection(nc, ctx, x, y_dram, bo, mod_dram, x1_dram, wo_raw, h2_hi, h2lo_dram, modT, ident,
                                 wo_loaded, wg_t, wu_t, shared, h2_lo0, gu_loaded, lo0_loaded)
            stage_gate_up(nc, ctx, wg_t, wu_t, h2_hi, h2_lo0, h2lo_dram, inter_dram, shared,
                          gu_loaded, lo0_loaded, wd_t, down_loaded)
        stage_down(nc, ctx, wd_t, mod_dram, x1_dram, inter_dram, out, shared[0], h2_hi0, down_loaded)


def kernel(**inputs):
    import numpy as np
    import concourse.bacc as bacc
    from concourse.bass_utils import run_bass_kernel_spmd

    def by_tiles(w):
        w = np.asarray(w)
        return np.ascontiguousarray(w.reshape(w.shape[0] // P, P, w.shape[1] // P, P).transpose(0, 3, 2, 1))

    arrays = {
        "x": inputs["L0_attn_x"],
        "wq_t": by_tiles(inputs["L0_attn_Wq"]),
        "wk_t": by_tiles(inputs["L0_attn_Wk"]),
        "wv_t": by_tiles(inputs["L0_attn_Wv"]),
        "wo_t": np.asarray(inputs["L0_attn_Wo"]).T.reshape(FT, P, D),
        "bo": inputs["L0_attn_bo"],
        "wg_t": np.asarray(inputs["L0_ffn_w_gate"]).T,
        "wu_t": np.asarray(inputs["L0_ffn_w_up"]).T,
        "wd_t": np.asarray(inputs["L0_ffn_w_down"]).T,
        "c": inputs["L0_c"],
        "wmod": inputs["L0_wmod"],
    }
    arrays = {f"in_{k}": np.ascontiguousarray(v) for k, v in arrays.items()}
    nc = bacc.Bacc("TRN2", target_bir_lowering=False, num_devices=1)
    args = [nc.dram_tensor(n, a.shape, mybir.dt.from_np(a.dtype), kind="ExternalInput").ap() for n, a in arrays.items()]
    result = nc.dram_tensor("out_dram", (1, T, D), F32, kind="ExternalOutput").ap()
    build(nc, *args, result)
    r = run_bass_kernel_spmd(nc, [arrays], core_ids=[0])
    return r.results[0]["out_dram"]
```
